# Optimizing a Trainium2 kernel written in Bass

```python
import numpy as np
import jax
import jax.numpy as jnp

def _softmax(x, axis=-1):
    return jax.nn.softmax(x, axis=axis)
def _gelu(x):
    return jax.nn.gelu(x, approximate=True)
def _silu(x):
    return jax.nn.silu(x)
def _sigmoid(x):
    return jax.nn.sigmoid(x)
def _layernorm(x, axis=-1, eps=1e-5):
    m = jnp.mean(x, axis=axis, keepdims=True)
    v = jnp.var(x, axis=axis, keepdims=True)
    return (x - m) / jnp.sqrt(v + eps)
def _scatter_add(tgt, idx, src, axis=0):
    return tgt.at[idx].add(src)
def _segment_sum(src, seg, n):
    return jax.ops.segment_sum(src, seg, n)

kernel_name = 'mk_rec_standalone_d1_rec_6c5955'

def setup_inputs(seed: int = 0):
    np.random.seed(seed)
    _w = jnp.asarray
    def _rec_inputs():
        import jax
        import jax.numpy as jnp
        _rk = jax.random.key(seed)
        r_x = -0.000611745 + 1.00059 * jax.random.normal(jax.random.fold_in(_rk, 1), (1024, 39, 16), jnp.float32)
        return r_x
    r_x = _rec_inputs()
    def _L0_rec_setup():
        import jax, jax.numpy as jnp
        import numpy as np
        F0 = 39
        CIN_SIZES = [128, 128, 128]
        B, D = (4096, 16)

        def _cin_forward(x, weights, biases):
            x0 = x
            xk = x
            fields = [F0] + CIN_SIZES
            outs = []
            for idx, s in enumerate(CIN_SIZES):
                fk = fields[idx]
                w = weights[idx].reshape(F0, fk, s)
                out = jnp.einsum('bid,bjd,ijs->bsd', x0, xk, w) + biases[idx][None, :, None]
                outs.append(out)
                xk = out
            res = jnp.concatenate(outs[1:], axis=1)
            return jnp.sum(res, axis=-1)
        key = jax.random.key(seed)
        ks = jax.random.split(key, 7)
        fields = [F0] + CIN_SIZES
        inp = {'x': jax.random.normal(ks[0], (B, F0, D), dtype=jnp.float32)}
        for i, s in enumerate(CIN_SIZES):
            m = fields[i] * F0
            inp[f'w{i}'] = jax.random.normal(ks[1 + 2 * i], (m, s), dtype=jnp.float32) * (2.0 / (m + s)) ** 0.5
            inp[f'b{i}'] = jax.random.normal(ks[2 + 2 * i], (s,), dtype=jnp.float32) * 0.02
        return inp
    _L0_rec_all = _L0_rec_setup()
    _L0_rec_in = {k: v for k, v in _L0_rec_all.items() if k in ('w0', 'b0', 'w1', 'b1', 'w2', 'b2', )}
    del _L0_rec_all

    return {
        "r_x": r_x,
        "L0_rec_w0": _L0_rec_in["w0"],
        "L0_rec_b0": _L0_rec_in["b0"],
        "L0_rec_w1": _L0_rec_in["w1"],
        "L0_rec_b1": _L0_rec_in["b1"],
        "L0_rec_w2": _L0_rec_in["w2"],
        "L0_rec_b2": _L0_rec_in["b2"],
    }

def reference(r_x, L0_rec_w0, L0_rec_b0, L0_rec_w1, L0_rec_b1, L0_rec_w2, L0_rec_b2):
    import jax
    import jax.numpy as jnp
    def _L0_rec_ref(x, w0, b0, w1, b1, w2, b2):
        import jax, jax.numpy as jnp
        import numpy as np
        F0 = 39
        CIN_SIZES = [128, 128, 128]
        B, D = (4096, 16)

        def _cin_forward(x, weights, biases):
            x0 = x
            xk = x
            fields = [F0] + CIN_SIZES
            outs = []
            for idx, s in enumerate(CIN_SIZES):
                fk = fields[idx]
                w = weights[idx].reshape(F0, fk, s)
                out = jnp.einsum('bid,bjd,ijs->bsd', x0, xk, w) + biases[idx][None, :, None]
                outs.append(out)
                xk = out
            res = jnp.concatenate(outs[1:], axis=1)
            return jnp.sum(res, axis=-1)
        return _cin_forward(x, [w0, w1, w2], [b0, b1, b2])

    y = _L0_rec_ref(r_x, L0_rec_w0, L0_rec_b0, L0_rec_w1, L0_rec_b1, L0_rec_w2, L0_rec_b2)
    return y


_drawn_inputs = setup_inputs


def setup_inputs(seed=0):
    import zlib

    import numpy as np

    out = dict(_drawn_inputs(seed))
    spreads = {}
    factors = {'L0_rec_b0': 3.951}
    for name, (base, spread) in spreads.items():
        noise = np.random.default_rng([zlib.crc32(name.encode()), seed]).standard_normal(out[name].shape)
        drawn = base * np.exp(spread * noise) if base else spread * noise
        out[name] = jnp.asarray(drawn.astype(out[name].dtype))
    for name, factor in factors.items():
        out[name] = (out[name] * factor).astype(out[name].dtype)
    return out
```

```python
import concourse.bass as bass
from concourse import mybir
from contextlib import ExitStack

B, F, D, S = 1024, 39, 16, 128
N = B * D
CH = 1024
NCH = N // CH
HB = 512
CB = CH // D
REP = 128 // F
R3 = REP * F
SHIFTS = (F + 1) // 2
NT = -(-SHIFTS // REP)
NG = CH // 128
GB = 128 // D
FX = F + 1
PB = 2 * CB
PAIRS = NCH // 2
LEAD = 4
ZR, ZHR, ZLR, XR = 4, 5, 5, 3


def rows_of(t):
    return min(REP, SHIFTS - REP * t) * F


def ring(size, n=F):
    short = next(k for k in range(n) if (n - k * (size - 1)) % size == 0)
    long = (n - short * (size - 1)) // size
    return [s for run in [size] * long + [size - 1] * short for s in range(run)]


def before(slots, i):
    for j in range(i - 1, i - 1 - len(slots), -1):
        if slots[j % len(slots)] == slots[i]:
            return j


ZS, ZHS, ZLS = ring(ZR), ring(ZHR), ring(ZLR)

DVE_LOW = [i for i in range(F) if i % 3 == 0]
POOL_LOW = [i for i in range(F) if i % 3 != 0]

PE_TURN = {2: 0, 3: 1}
PE_G = {6 + g: g for g in range(NG)}
PE_LAYER2 = {14: range(0, 13), 15: range(13, 26), 16: range(26, 39)}
PE_LAYER0 = {17 + 3 * t: t for t in range(NT)}
ACT_O1 = 2
ACT_TURN = {6: 0, 7: 1}
ACT_G = {10 + g: g for g in range(NG)}
ACT_Y2 = 20
ACT_X3 = {9: 0, 13: 1}
DVE_X3 = {11: 0, 15: 1}
DVE_PAIRS = {17 + 3 * t: t for t in range(NT)}


def cin_kernel(nc: bass.Bass, xr, xt, w0, b0, w1, b1, w2, b2, out):
    f32, f32r, bf16 = mybir.dt.float32, mybir.dt.float32r, mybir.dt.bfloat16
    ALU, ACT = mybir.AluOpType, mybir.ActivationFunctionType

    ctx = ExitStack()
    with ctx:
        def sb(name, shape, dt=f32):
            return ctx.enter_context(nc.sbuf_tensor(name, shape, dt))

        def sem(name):
            return ctx.enter_context(nc.semaphore(name))

        w1h = sb("w1h", [128, F, S], f32r)
        w1l = sb("w1l", [128, F, S], f32r)
        w2s = sb("w2s", [128, F, S])
        w0s = sb("w0s", [R3, NT, S])
        bias = sb("bias", [128, 3])
        b2x = sb("b2x", [128, 1])
        pick = sb("pick", [R3, F, S], bf16)
        one_hot = sb("one_hot", [R3, F])
        minus = sb("minus", [R3, 2])
        ident = sb("ident", [128, 128])
        ones = sb("ones", [128, NG])
        xa = sb("xa", [R3, CH])
        xs = sb("xs", [R3, XR, CH])
        part = sb("part", [R3, CH], bf16)
        rest = sb("rest", [R3, CH])
        x3 = sb("x3", [R3, 2, CH], bf16)
        o0 = sb("o0", [128, 2, CH])
        z = sb("z", [128, ZR, CH])
        zh = sb("zh", [128, ZHR, CH], f32r)
        zl = sb("zl", [128, ZLR, CH], f32r)
        o1 = sb("o1", [128, CH])
        o1t = sb("o1t", [128, NG, 128])
        xd = sb("xd", [128, NG, GB, FX])
        gs = sb("gs", [128, FX, PB])
        y2 = sb("y2", [128, PB])
        w1raw = gs[:, 0:F, 0:S]
        w0b = z[0:R3, 0, 0:NT * S].rearrange("p (t s) -> p t s", t=NT)

        xb_p = [ctx.enter_context(nc.psum_tensor(f"xb{i}", [128, CH], f32)) for i in range(2)]
        o1_p = ctx.enter_context(nc.psum_tensor("o1_p", [128, CH], f32))
        misc = ctx.enter_context(nc.psum_tensor("misc", [128, 2, HB], f32))

        w1_in, w2_in, w0_in, bias_in = sem("w1_in"), sem("w2_in"), sem("w0_in"), sem("bias_in")
        ones_in, xa_in, xd_in = sem("ones_in"), sem("xa_in"), sem("xd_in")
        xs_in = [sem(f"xs_in{k}") for k in range(XR)]
        zeroed, consts, picks, ones_set = sem("zeroed"), sem("consts"), sem("picks"), sem("ones_set")
        w0_ready, w1h_ready, w1l_ready, b2_ready = sem("w0_ready"), sem("w1h_ready"), sem("w1l_ready"), sem("b2_ready")
        part_ready, rest_ready, x3_ready = sem("part_ready"), sem("rest_ready"), sem("x3_ready")
        pairs_ready, pairs_used, o0_ready = sem("pairs_ready"), sem("pairs_used"), sem("o0_ready")
        xb_ready, z_ready, zh_ready = sem("xb_ready"), sem("z_ready"), sem("zh_ready")
        low_dve, low_pool, unit_used = sem("low_dve"), sem("low_pool"), sem("unit_used")
        half_summed, o1_ready, turned, o1t_ready = sem("half_summed"), sem("o1_ready"), sem("turned"), sem("o1t_ready")
        gs_free = sem("gs_free")
        g_summed, g_ready, y2_summed, y2_ready = sem("g_summed"), sem("g_ready"), sem("y2_summed"), sem("y2_ready")
        stored = sem("stored")

        def chunks(eng, chunk):
            chunk(0, 0, None)
            with eng.Fori(0, PAIRS - 1) as p:
                chunk(2 * p + 1, 1, p)
                chunk(2 * p + 2, 0, p)
            chunk(NCH - 1, 1, PAIRS - 1)

        def await_count(eng, sem_, per, c, k):
            if isinstance(c, int) and c * per + k <= 0:
                return
            eng.wait_ge(sem_, c * per + k)

        def await_low(eng, c, i):
            if i < 0:
                if isinstance(c, int) and c == 0:
                    return
                c, i = c - 1, i + F
            if i in DVE_LOW:
                await_count(eng, low_dve, len(DVE_LOW), c, DVE_LOW.index(i) + 1)
            else:
                await_count(eng, low_pool, len(POOL_LOW), c, POOL_LOW.index(i) + 1)

        def first(c):
            return isinstance(c, int) and c == 0

        def last(c):
            return isinstance(c, int) and c == NCH - 1

        def make_low(eng, c, i, done):
            await_count(eng, zh_ready, F, c, i + 1)
            await_count(eng, unit_used, F, c, before(ZLS, i) + 1)
            eng.tensor_tensor(zl[:, ZLS[i], :], z[:, ZS[i], :], zh[:, ZHS[i], :].bitcast(f32),
                              ALU.subtract).then_inc(done, 1)

        block = ctx.enter_context(nc.Block())

        @block.sync
        def _(sp):
            def load_xa(c):
                if not first(c):
                    sp.wait_ge(pairs_ready, c * NT)
                for r in range(REP):
                    sp.dma_start(xa[F * r:F * r + F, :], xr[0:F, bass.ds(c * CH, CH)]).then_inc(xa_in, 16)

            def load_shifts(c, tiles):
                for t in tiles:
                    prior = t - XR if t >= XR else max(u for u in range(NT) if u % XR == t) - NT
                    await_count(sp, pairs_used, NT, c, prior + 1)
                    for r in range(rows_of(t) // F):
                        k = REP * t + r
                        sp.dma_start(xs[F * r:F * r + F, t % XR, :], xr[k:k + F, bass.ds(c * CH, CH)])\
                          .then_inc(xs_in[t % XR], 16)

            def load_diagonal(c):
                if not first(c):
                    sp.wait_ge(g_summed, c * NG)
                src = xt[bass.ds(c * CH, CH), :].rearrange("(g b d) f -> b d g f", g=NG, b=GB)
                for b in range(GB):
                    sp.dma_start(xd[D * b:D * b + D, :, b, 0:F], src[b]).then_inc(xd_in, 16)

            def store(pair):
                sp.wait_ge(g_ready, (pair + 1) * 2 * NG)
                sp.dma_start(out[0:S, bass.ds(pair * PB, PB)], gs[:, F, :]).then_inc(stored, 16)
                sp.wait_ge(y2_ready, pair + 1)
                sp.dma_start(out[S:2 * S, bass.ds(pair * PB, PB)], y2[:, :]).then_inc(stored, 16)
                sp.wait_ge(stored, (pair + 1) * 32)
                sp.sem_inc(gs_free, 1)

            def step(c):
                if not last(c):
                    load_xa(c + 1)
                    load_shifts(c + 1, range(XR))
                load_diagonal(c)
                if not last(c):
                    load_shifts(c + 1, range(XR, NT))

            load_xa(0)
            load_shifts(0, range(XR))
            sp.dma_start(w1raw, w1.rearrange("(i j) s -> j i s", j=128)).then_inc(w1_in, 16)
            load_shifts(0, range(XR, NT))
            sp.wait_ge(ones_set, 2)
            with nc.allow_non_contiguous_dma(reason="single ones, once"):
                for b in range(GB):
                    sp.dma_start(xd[D * b:D * b + D, :, b, F:FX], ones[0:D, :]).then_inc(ones_in, 16)
            step(0)
            with sp.Fori(0, PAIRS - 1) as p:
                step(2 * p + 1)
                step(2 * p + 2)
                store(p)
            step(NCH - 1)
            store(PAIRS - 1)
            sp.wait_ge(stored, NCH * 16)

        @block.gpsimd
        def _(pool):
            pool.memset(w0b, 0.0).then_inc(zeroed, 1)
            pool.memset(ones[:, :], 1.0).then_inc(ones_set, 1)
            pool.memset(xd[:, :, :, :], 0.0).then_inc(ones_set, 1)
            pool.memset(ident[:, :], 0.0).then_inc(consts, 1)
            pool.memset(one_hot[:, :], 0.0).then_inc(consts, 1)
            pool.memset(minus[:, :], -1.0).then_inc(consts, 1)
            pool.wait_ge(consts, 3)
            for r in range(REP):
                pool.affine_select(out=one_hot[:, :], in_=one_hot[:, :], compare_op=ALU.not_equal, fill=1.0,
                                   base=-F * r, pattern=[[-1, F]], channel_multiplier=1).then_inc(consts, 1)
                pool.wait_ge(consts, 4 + r)
            for r in range(2):
                pool.affine_select(out=minus[:, r:r + 1], in_=minus[:, r:r + 1], compare_op=ALU.is_ge, fill=0.0,
                                   base=-F * (r + 1), pattern=[[0, 1]], channel_multiplier=1).then_inc(consts, 1)
            pool.affine_select(out=ident[:, :], in_=ident[:, :], compare_op=ALU.not_equal, fill=1.0,
                               base=0, pattern=[[-1, 128]], channel_multiplier=1).then_inc(consts, 1)

            def chunk(c, par, pair):
                for i in POOL_LOW:
                    make_low(pool, c, i, low_pool)

            chunks(pool, chunk)

        @block.scalar
        def _(act):
            with nc.allow_non_contiguous_dma(reason="short bias columns"):
                for k, b in enumerate((b0, b1, b2)):
                    act.dma_start(bias[:, k:k + 1], b.rearrange("(s a) -> s a", a=1)).then_inc(bias_in, 16)
            act.wait_ge(zeroed, 1)
            for k in range(SHIFTS):
                t, p = k // REP, F * (k % REP)
                n = F - k
                act.dma_start(w0s[p:p + n, t, :], w0[k:k + (n - 1) * FX + 1:FX, :]).then_inc(w0_in, 16)
                if k:
                    act.dma_start(w0s[p + n:p + F, t, :],
                                  w0[n * FX + k - F:n * FX + k - F + (k - 1) * FX + 1:FX, :]).then_inc(w0_in, 16)
                    act.dma_start(w0b[p:p + n, t, :], w0[F * k:F * k + (n - 1) * FX + 1:FX, :]).then_inc(w0_in, 16)
                    act.dma_start(w0b[p + n:p + F, t, :],
                                  w0[n:n + (k - 1) * FX + 1:FX, :]).then_inc(w0_in, 16)
            act.dma_start(w2s[:, :, :], w2.rearrange("(i j) s -> j i s", j=128)).then_inc(w2_in, 16)

            def take_part(c, k):
                if k == 0:
                    act.wait_ge(xa_in, (c + 1) * 16 * REP)
                    act.activation(part[:, :], xa[:, :], ACT.Copy).then_inc(part_ready, 1)
                else:
                    act.wait_ge(rest_ready, c + 1)
                    act.activation(part[:, :], rest[:, :], ACT.Copy).then_inc(part_ready, 1)

            def finish_o0(c, par):
                act.wait_ge(pairs_used, (c + 1) * NT)
                for h in range(2):
                    act.activation(o0[:, par, h * HB:(h + 1) * HB], misc[:, h, :], ACT.Identity,
                                   bias=bias[:, 0:1]).then_inc(o0_ready, 1)

            def finish_o1(c):
                for h in range(2):
                    if h == 0:
                        act.wait_ge(half_summed, c + 1)
                    else:
                        act.wait_ge(unit_used, (c + 1) * F)
                    act.activation(o1[:, h * HB:(h + 1) * HB], o1_p[:, h * HB:(h + 1) * HB], ACT.Identity,
                                   bias=bias[:, 1:2]).then_inc(o1_ready, 1)

            def copy_turned(c, h):
                act.wait_ge(turned, 2 * c + h + 1)
                act.activation(o1t[:, 4 * h:4 * h + 4, :].rearrange("p g j -> p (g j)"), misc[:, h, :],
                               ACT.Copy).then_inc(o1t_ready, 1)

            def copy_g(c, par, pair, g):
                if g == 0 and par == 0:
                    act.wait_ge(gs_free, pair + 1)
                act.wait_ge(g_summed, c * NG + g + 1)
                at = par * CB + g * GB
                act.activation(gs[:, :, at:at + GB], misc[:, g % 2, 0:GB * FX].rearrange("p (b f) -> p f b", b=GB),
                               ACT.Copy).then_inc(g_ready, 1)

            def finish_y2(pair):
                act.wait_ge(y2_summed, pair + 1)
                act.activation(y2[:, :], misc[:, 0, 0:PB], ACT.Identity, bias=b2x[:, 0:1]).then_inc(y2_ready, 1)

            def chunk(c, par, pair):
                for i in range(F):
                    await_count(act, z_ready, F, c, i + 1)
                    await_count(act, unit_used, F, c, before(ZHS, i) + 1)
                    act.activation(zh[:, ZHS[i], :], z[:, ZS[i], :], ACT.Copy).then_inc(zh_ready, 1)
                    if not first(c):
                        if i == ACT_O1:
                            finish_o1(c - 1)
                        if i in ACT_TURN:
                            copy_turned(c - 1, ACT_TURN[i])
                        if i in ACT_G:
                            copy_g(c - 1, 1 - par, pair, ACT_G[i])
                        if i == ACT_Y2 and par == 0:
                            finish_y2(pair)
                    if not last(c) and i in ACT_X3:
                        take_part(c + 1, ACT_X3[i])
                if not last(c):
                    finish_o0(c + 1, 1 - par)

            act.wait_ge(bias_in, 48)
            take_part(0, 0)
            act.wait_ge(w1_in, 16)
            for q in range(3):
                act.activation(w1h[:, 13 * q:13 * q + 13, :], w1raw[:, 13 * q:13 * q + 13, :], ACT.Copy)\
                   .then_inc(w1h_ready, 1)
                if q == 0:
                    take_part(0, 1)
            finish_o0(0, 0)
            chunks(act, chunk)
            finish_o1(NCH - 1)
            for h in range(2):
                copy_turned(NCH - 1, h)
            for g in range(NG):
                copy_g(NCH - 1, 1, PAIRS - 1, g)
            finish_y2(PAIRS - 1)

        @block.vector
        def _(dve):
            def make_rest(c, k):
                dve.wait_ge(part_ready, 2 * c + k + 1)
                if k == 0:
                    dve.scalar_tensor_tensor(out=rest[:, :], in0=part[:, :], scalar=minus[:, 0:1], in1=xa[:, :],
                                             op0=ALU.mult, op1=ALU.add).then_inc(rest_ready, 1)

            def make_x3(c, par):
                dve.wait_ge(part_ready, 2 * c + 2)
                dve.scalar_tensor_tensor(out=x3[:, par, :], in0=part[:, :], scalar=minus[:, 1:2], in1=rest[:, :],
                                         op0=ALU.mult, op1=ALU.add).then_inc(x3_ready, 1)

            def make_pairs(c, t):
                a = 16 * REP
                held = [u for u in range(NT) if u % XR == t % XR]
                counts = [16 * (rows_of(u) // F) for u in held]
                await_count(dve, xs_in[t % XR], sum(counts), c, sum(counts[:held.index(t) + 1]))
                if t == 0:
                    dve.wait_ge(xa_in, c * a + a)
                p = rows_of(t)
                dve.tensor_tensor(xs[0:p, t % XR, :], xs[0:p, t % XR, :], xa[0:p, :], ALU.mult)\
                   .then_inc(pairs_ready, 1)

            def chunk(c, par, pair):
                for i in range(F):
                    await_count(dve, xb_ready, F, c, i + 1)
                    if i == 0:
                        dve.wait_ge(o0_ready, 2 * c + 2)
                    u = before(ZS, i)
                    await_count(dve, zh_ready, F, c, u + 1)
                    await_low(dve, c, u)
                    dve.tensor_tensor(z[:, ZS[i], :], xb_p[(i + par) % 2][:, :], o0[:, par, :], ALU.mult)\
                       .then_inc(z_ready, 1)
                    if i - 2 in DVE_LOW:
                        make_low(dve, c, i - 2, low_dve)
                    if not last(c):
                        if i in DVE_X3 and DVE_X3[i] == 0:
                            make_rest(c + 1, 0)
                        if i in DVE_X3 and DVE_X3[i] == 1:
                            make_x3(c + 1, 1 - par)
                        if i in DVE_PAIRS:
                            make_pairs(c + 1, DVE_PAIRS[i])

            dve.wait_ge(bias_in, 48)
            dve.tensor_scalar(b2x[:, :], bias[:, 2:3], float(D), None, ALU.mult).then_inc(b2_ready, 1)
            dve.wait_ge(consts, 4 + REP + 1)
            dve.tensor_copy(pick[:, :, :], one_hot[:, :].unsqueeze(2).broadcast_to([R3, F, S])).then_inc(picks, 1)
            make_rest(0, 0)
            full = NT - 1
            dve.wait_ge(w0_in, 16 * (1 + 4 * (SHIFTS - 1)))
            dve.tensor_tensor(w0s[:, 0:full, :], w0s[:, 0:full, :], w0b[:, 0:full, :], ALU.add).then_inc(w0_ready, 1)
            p = rows_of(full)
            dve.tensor_tensor(w0s[0:p, full, :], w0s[0:p, full, :], w0b[0:p, full, :], ALU.add).then_inc(w0_ready, 1)
            make_x3(0, 0)
            for t in range(NT):
                make_pairs(0, t)
            for q in range(3):
                dve.wait_ge(w1h_ready, q + 1)
                dve.tensor_tensor(w1l[:, 13 * q:13 * q + 13, :], w1raw[:, 13 * q:13 * q + 13, :],
                                  w1h[:, 13 * q:13 * q + 13, :].bitcast(f32), ALU.subtract).then_inc(w1l_ready, 1)
            dve.wait_ge(w1l_ready, 3)
            dve.sem_inc(gs_free, 1)
            dve.wait_ge(w0_ready, 2)
            chunks(dve, chunk)

        @block.tensor
        def _(pe):
            def spread(c, par, i):
                if i == 0:
                    pe.wait_ge(x3_ready, c + 1)
                await_count(pe, z_ready, F, c, i - 1)
                for h in range(2):
                    mm = pe.matmul(xb_p[(i + par) % 2][:, h * HB:(h + 1) * HB], pick[:, i, :],
                                   x3[:, par, h * HB:(h + 1) * HB], start=True, stop=True)
                mm.then_inc(xb_ready, 1)

            def layer1(c, i):
                at = [slice(h * HB, (h + 1) * HB) for h in range(2)]
                start, stop = i == 0, i == F - 1
                await_count(pe, zh_ready, F, c, i + 1)
                if first(c) and i % 13 == 0:
                    pe.wait_ge(w1l_ready, i // 13 + 1)

                def high(h):
                    if start and not first(c):
                        pe.wait_ge(o1_ready, 2 * c - 1 + h)
                    pe.matmul(o1_p[:, at[h]], w1h[:, i, :], zh[:, ZHS[i], at[h]], start=start, stop=False)
                    pe.matmul(o1_p[:, at[h]], w1l[:, i, :], zh[:, ZHS[i], at[h]], start=False, stop=False)

                def low(h):
                    return pe.matmul(o1_p[:, at[h]], w1h[:, i, :], zl[:, ZLS[i], at[h]], start=False, stop=stop)

                high(0)
                if stop:
                    await_low(pe, c, i)
                    low(0).then_inc(half_summed, 1)
                    high(1)
                else:
                    high(1)
                    await_low(pe, c, i)
                    low(0)
                low(1).then_inc(unit_used, 1)

            def layer0(c, t, at_start):
                p = rows_of(t)
                pe.wait_ge(pairs_ready, c * NT + t + 1)
                if t == 0 and not at_start:
                    pe.wait_ge(g_ready, (c - 1) * NG)
                for h in range(2):
                    mm = pe.matmul(misc[:, h, :], w0s[0:p, t, :], xs[0:p, t % XR, h * HB:(h + 1) * HB],
                                   start=(t == 0), stop=(t == NT - 1))
                mm.then_inc(pairs_used, 1)

            def turn(c, h):
                pe.wait_ge(o1_ready, 2 * c + h + 1)
                if h == 0 and not last(c):
                    pe.wait_ge(o0_ready, 2 * c + 4)
                for g in range(4):
                    k = (4 * h + g) * 128
                    mm = pe.transpose(misc[:, h, g * 128:(g + 1) * 128], o1[:, k:k + 128], ident[:, :])
                mm.then_inc(turned, 1)

            def g_sum(c, g):
                if g == 0:
                    pe.wait_ge(o1t_ready, 2 * c + 2)
                    pe.wait_ge(xd_in, (c + 1) * 16 * GB)
                if g >= 2:
                    pe.wait_ge(g_ready, c * NG + g - 1)
                pe.matmul(misc[:, g % 2, 0:GB * FX], o1t[:, g, :], xd[:, g, :, :].rearrange("p b f -> p (b f)"),
                          start=True, stop=True).then_inc(g_summed, 1)

            def layer2(c, fields):
                if fields[0] == 0:
                    pe.wait_ge(g_ready, (c + 1) * NG)
                for i in fields:
                    mm = pe.matmul(misc[:, 0, 0:PB], w2s[:, i, :], gs[:, i, :], start=(i == 0), stop=(i == F - 1))
                if fields[-1] == F - 1:
                    mm.then_inc(y2_summed, 1)

            def chunk(c, par, pair):
                for i in range(F):
                    if i + LEAD < F:
                        spread(c, par, i + LEAD)
                    elif not last(c):
                        spread(c + 1, 1 - par, i + LEAD - F)
                    layer1(c, i)
                    if not first(c):
                        if i in PE_TURN:
                            turn(c - 1, PE_TURN[i])
                        if i in PE_G:
                            g_sum(c - 1, PE_G[i])
                        if par == 0 and i in PE_LAYER2:
                            layer2(c - 1, PE_LAYER2[i])
                    if not last(c) and i in PE_LAYER0:
                        if PE_LAYER0[i] == 0 and par == 0 and not first(c):
                            pe.wait_ge(y2_ready, pair + 1)
                        layer0(c + 1, PE_LAYER0[i], first(c))

            pe.wait_ge(consts, 4 + REP + 2)
            pe.wait_ge(w0_ready, 2)
            for t in range(NT):
                layer0(0, t, True)
            pe.wait_ge(picks, 1)
            for i in range(LEAD):
                spread(0, 0, i)
            pe.wait_ge(ones_in, 16 * GB)
            pe.wait_ge(w2_in, 16)
            chunks(pe, chunk)
            for h in range(2):
                turn(NCH - 1, h)
            for g in range(NG):
                g_sum(NCH - 1, g)
            layer2(NCH - 1, range(F))


def kernel(**inputs):
    import numpy as np
    import concourse.bacc as bacc
    from concourse.bass_utils import run_bass_kernel_spmd

    x = np.asarray(inputs["r_x"])
    by_field = np.ascontiguousarray(x.transpose(1, 0, 2).reshape(F, N))
    arrays = {
        "xr": np.concatenate([by_field, by_field[:SHIFTS]]),
        "xt": np.ascontiguousarray(x.transpose(0, 2, 1).reshape(N, F)),
    }
    for k in range(3):
        arrays[f"w{k}"] = np.ascontiguousarray(inputs[f"L0_rec_w{k}"])
        arrays[f"b{k}"] = np.ascontiguousarray(inputs[f"L0_rec_b{k}"])
    nc = bacc.Bacc("TRN2", target_bir_lowering=False, num_devices=1)
    ap = {n: nc.dram_tensor(n, a.shape, mybir.dt.float32, kind="ExternalInput").ap() for n, a in arrays.items()}
    out = nc.dram_tensor("out", (2 * S, B), mybir.dt.float32, kind="ExternalOutput").ap()
    cin_kernel(nc, ap["xr"], ap["xt"], ap["w0"], ap["b0"], ap["w1"], ap["b1"], ap["w2"], ap["b2"], out)
    got = run_bass_kernel_spmd(nc, [arrays], core_ids=[0])
    return np.ascontiguousarray(got.results[0]["out"].T)
```

```python
import concourse.bass as bass
from concourse import mybir
from contextlib import ExitStack

B, F, D, S = 1024, 39, 16, 128
N = B * D
CH = 1024
NCH = N // CH
HB = 512
CB = CH // D
REP = 128 // F
R3 = REP * F
SHIFTS = (F + 1) // 2
NT = -(-SHIFTS // REP)
NG = CH // 128
GB = 128 // D
FX = F + 1
PB = 2 * CB
PAIRS = NCH // 2
LOW_LAG = 2
LEAD = 4
ZR, ZHR, ZLR, XR = 5, 6, 6, 2


def rows_of(t):
    return min(REP, SHIFTS - REP * t) * F


AFTER = dict(zip((20, 22, 24, 26, 28, 30, 32), range(NT)))
SEQ = [u for i in range(F) for u in [("o1", i)] + ([("o0", AFTER[i])] if i in AFTER else [])]
U = len(SEQ)
FIELD = [SEQ.index(("o1", i)) for i in range(F)]
TILE = [SEQ.index(("o0", t)) for t in range(NT)]
ALL = range(U)
DVE_LOW = FIELD[0::3]
POOL_LOW = [k for k in FIELD if k not in DVE_LOW]


def ring(size, units):
    n = len(units)
    short = next(k for k in range(n) if (n - k * (size - 1)) % size == 0)
    long = (n - short * (size - 1)) // size
    return dict(zip(units, (s for run in [size] * long + [size - 1] * short for s in range(run))))


ZS, ZHS, ZLS = ring(ZR, ALL), ring(ZHR, FIELD), ring(ZLR, FIELD)


def present(c):
    return TILE if isinstance(c, int) and c < 0 else FIELD if isinstance(c, int) and c == NCH - 1 else list(ALL)


def count(c, k, among=ALL):
    before_first = len([u for u in TILE if u in among])
    rank = len([u for u in present(c) if u in among and u <= k])
    return rank if isinstance(c, int) and c < 0 else before_first + c * len(among) + rank


def holder(slots, c, k):
    held = [u for u in present(c) if u < k and slots.get(u) == slots[k]]
    if held:
        return c, held[-1]
    if isinstance(c, int) and c < 0:
        return None
    held = [u for u in present(c - 1) if slots.get(u) == slots[k]]
    return (c - 1, held[-1]) if held else None


PE_TURN = {1: 0, 2: 1}
PE_G = {4 + g: g for g in range(NG)}
PE_LAYER2 = {12 + n: range(6 * n, min(6 * n + 6, F)) for n in range(7)}
ACT_O1 = 2
ACT_TURN = {5: 0, 6: 1}
ACT_G = {8 + g: g for g in range(NG)}
ACT_Y2 = 22
ACT_X3 = {17: 0, 21: 1}
ACT_O0 = 36
DVE_X3 = {19: 0, 23: 1}


def cin_kernel(nc: bass.Bass, xr, xt, w0, b0, w1, b1, w2, b2, out):
    f32, f32r, bf16 = mybir.dt.float32, mybir.dt.float32r, mybir.dt.bfloat16
    ALU, ACT = mybir.AluOpType, mybir.ActivationFunctionType

    ctx = ExitStack()
    with ctx:
        def sb(name, shape, dt=f32):
            return ctx.enter_context(nc.sbuf_tensor(name, shape, dt))

        def sem(name):
            return ctx.enter_context(nc.semaphore(name))

        w1h = sb("w1h", [128, F, S], f32r)
        w1l = sb("w1l", [128, F, S], f32r)
        w2s = sb("w2s", [128, F, S])
        w0s = sb("w0s", [R3, NT, S])
        bias = sb("bias", [128, 3])
        b2x = sb("b2x", [128, 1])
        pick = sb("pick", [R3, F, S], bf16)
        one_hot = sb("one_hot", [R3, F])
        minus = sb("minus", [R3, 2])
        ident = sb("ident", [128, 128])
        ones = sb("ones", [128, NG])
        xa = sb("xa", [R3, CH])
        xs = sb("xs", [R3, XR, CH])
        x3 = sb("x3", [R3, 2, CH], bf16)
        o0 = sb("o0", [128, 2, CH])
        z = sb("z", [128, ZR, CH])
        zh = sb("zh", [128, ZHR, CH], f32r)
        zl = sb("zl", [128, ZLR, CH], f32r)
        o1 = sb("o1", [128, CH])
        o1t = sb("o1t", [128, NG, 128])
        rest = o1[0:R3, :]
        part = o1t[0:R3, 0:NG // 2, :].rearrange("p g j -> p (g j)").bitcast(bf16)
        xd = sb("xd", [128, NG, GB, FX])
        gs = sb("gs", [128, FX, PB])
        y2 = sb("y2", [128, PB])
        w1raw = gs[:, 0:F, 0:S]
        w0b = o0[0:R3, 1, 0:NT * S].rearrange("p (t s) -> p t s", t=NT)

        xb_p = [ctx.enter_context(nc.psum_tensor(f"xb{i}", [128, CH], f32)) for i in range(2)]
        o1_p = ctx.enter_context(nc.psum_tensor("o1_p", [128, CH], f32))
        misc = ctx.enter_context(nc.psum_tensor("misc", [128, 2, HB], f32))

        w1_in = [sem(f"w1_in{q}") for q in range(3)]
        w2_in, w0_in, bias_in = sem("w2_in"), sem("w0_in"), sem("bias_in")
        ones_in, xa_in, xd_in = sem("ones_in"), sem("xa_in"), sem("xd_in")
        xs_in = [sem(f"xs_in{k}") for k in range(XR)]
        zeroed, consts, picks, ones_set = sem("zeroed"), sem("consts"), sem("picks"), sem("ones_set")
        w0_ready, w1h_ready, b2_ready = sem("w0_ready"), sem("w1h_ready"), sem("b2_ready")
        w1l_ready = [sem(f"w1l_ready{q}") for q in range(3)]
        part_ready, rest_ready, x3_ready = sem("part_ready"), sem("rest_ready"), sem("x3_ready")
        o0_ready = sem("o0_ready")
        xb_ready, z_ready, zh_ready = sem("xb_ready"), sem("z_ready"), sem("zh_ready")
        low_dve, low_pool, unit_used = sem("low_dve"), sem("low_pool"), sem("unit_used")
        half_summed, o1_ready, turned, o1t_ready = sem("half_summed"), sem("o1_ready"), sem("turned"), sem("o1t_ready")
        gs_free = sem("gs_free")
        g_summed, g_ready, y2_summed, y2_ready = sem("g_summed"), sem("g_ready"), sem("y2_summed"), sem("y2_ready")
        stored = sem("stored")

        def chunks(eng, chunk):
            chunk(0, 0, None)
            with eng.Fori(0, PAIRS - 1) as p:
                chunk(2 * p + 1, 1, p)
                chunk(2 * p + 2, 0, p)
            chunk(NCH - 1, 1, PAIRS - 1)

        def await_unit(eng, sem_, unit, among=ALL):
            if unit is not None:
                eng.wait_ge(sem_, count(*unit, among))

        def await_low(eng, unit):
            if unit is not None:
                on_dve = unit[1] in DVE_LOW
                await_unit(eng, low_dve if on_dve else low_pool, unit, DVE_LOW if on_dve else POOL_LOW)

        def first(c):
            return isinstance(c, int) and c == 0

        def last(c):
            return isinstance(c, int) and c == NCH - 1

        def make_low(eng, c, k, done):
            await_unit(eng, zh_ready, (c, k), FIELD)
            await_unit(eng, unit_used, holder(ZLS, c, k))
            eng.tensor_tensor(zl[:, ZLS[k], :], z[:, ZS[k], :], zh[:, ZHS[k], :].bitcast(f32),
                              ALU.subtract).then_inc(done, 1)

        def low_weights(eng, q):
            eng.wait_ge(w1h_ready, q + 1)
            eng.tensor_tensor(w1l[:, 13 * q:13 * q + 13, :], w1raw[:, 13 * q:13 * q + 13, :],
                              w1h[:, 13 * q:13 * q + 13, :].bitcast(f32), ALU.subtract).then_inc(w1l_ready[q], 1)

        block = ctx.enter_context(nc.Block())

        @block.sync
        def _(sp):
            def load_xa(c):
                if not first(c):
                    await_unit(sp, z_ready, (c - 2, TILE[-1]))
                for r in range(REP):
                    sp.dma_start(xa[F * r:F * r + F, :], xr[0:F, bass.ds(c * CH, CH)]).then_inc(xa_in, 16)

            def load_shifts(c, tiles):
                for t in tiles:
                    user = (c - 1, TILE[t - XR]) if t >= XR else \
                        None if first(c) else (c - 2, TILE[max(u for u in range(NT) if u % XR == t)])
                    await_unit(sp, z_ready, user)
                    for r in range(rows_of(t) // F):
                        k = REP * t + r
                        sp.dma_start(xs[F * r:F * r + F, t % XR, :], xr[k:k + F, bass.ds(c * CH, CH)])\
                          .then_inc(xs_in[t % XR], 16)

            def load_diagonal(c):
                if not first(c):
                    sp.wait_ge(g_summed, c * NG)
                src = xt[bass.ds(c * CH, CH), :].rearrange("(g b d) f -> b d g f", g=NG, b=GB)
                for b in range(GB):
                    sp.dma_start(xd[D * b:D * b + D, :, b, 0:F], src[b]).then_inc(xd_in, 16)

            def store(pair):
                sp.wait_ge(g_ready, (pair + 1) * 2 * NG)
                sp.dma_start(out[0:S, bass.ds(pair * PB, PB)], gs[:, F, :]).then_inc(stored, 16)
                sp.wait_ge(y2_ready, pair + 1)
                sp.dma_start(out[S:2 * S, bass.ds(pair * PB, PB)], y2[:, :]).then_inc(stored, 16)
                sp.wait_ge(stored, (pair + 1) * 32)
                sp.sem_inc(gs_free, 1)

            def step(c):
                if not last(c):
                    load_xa(c + 1)
                    load_shifts(c + 1, range(XR))
                load_diagonal(c)
                if not last(c):
                    load_shifts(c + 1, range(XR, NT))

            load_xa(0)
            load_shifts(0, range(XR))
            with nc.allow_non_contiguous_dma(reason="short bias columns"):
                for k, b in enumerate((b0, b1, b2)):
                    sp.dma_start(bias[:, k:k + 1], b.rearrange("(s a) -> s a", a=1)).then_inc(bias_in, 16)
            load_shifts(0, range(XR, NT))
            sp.wait_ge(ones_set, 2)
            with nc.allow_non_contiguous_dma(reason="single ones, once"):
                for b in range(GB):
                    sp.dma_start(xd[D * b:D * b + D, :, b, F:FX], ones[0:D, :]).then_inc(ones_in, 16)
            sp.dma_start(w2s[:, :, :], w2.rearrange("(i j) s -> j i s", j=128)).then_inc(w2_in, 16)
            for q in range(3):
                sp.wait_ge(w1l_ready[q], 1)
            sp.sem_inc(gs_free, 1)
            step(0)
            with sp.Fori(0, PAIRS - 1) as p:
                step(2 * p + 1)
                step(2 * p + 2)
                store(p)
            step(NCH - 1)
            store(PAIRS - 1)
            sp.wait_ge(stored, NCH * 16)

        @block.gpsimd
        def _(pool):
            pool.memset(w0b, 0.0).then_inc(zeroed, 1)
            pool.memset(ones[:, :], 1.0).then_inc(ones_set, 1)
            pool.memset(xd[:, :, :, :], 0.0).then_inc(ones_set, 1)
            pool.memset(ident[:, :], 0.0).then_inc(consts, 1)
            pool.memset(one_hot[:, :], 0.0).then_inc(consts, 1)
            pool.memset(minus[:, :], -1.0).then_inc(consts, 1)
            pool.wait_ge(consts, 3)
            for r in range(REP):
                pool.affine_select(out=one_hot[:, :], in_=one_hot[:, :], compare_op=ALU.not_equal, fill=1.0,
                                   base=-F * r, pattern=[[-1, F]], channel_multiplier=1).then_inc(consts, 1)
                pool.wait_ge(consts, 4 + r)
            for r in range(2):
                pool.affine_select(out=minus[:, r:r + 1], in_=minus[:, r:r + 1], compare_op=ALU.is_ge, fill=0.0,
                                   base=-F * (r + 1), pattern=[[0, 1]], channel_multiplier=1).then_inc(consts, 1)
            pool.affine_select(out=ident[:, :], in_=ident[:, :], compare_op=ALU.not_equal, fill=1.0,
                               base=0, pattern=[[-1, 128]], channel_multiplier=1).then_inc(consts, 1)

            pool.wait_ge(consts, 4 + REP)
            pool.tensor_copy(pick[:, :, :], one_hot[:, :].unsqueeze(2).broadcast_to([R3, F, S])).then_inc(picks, 1)
            for q in (1, 2):
                low_weights(pool, q)

            def chunk(c, par, pair):
                for k in POOL_LOW:
                    make_low(pool, c, k, low_pool)

            chunks(pool, chunk)

        @block.scalar
        def _(act):
            act.wait_ge(zeroed, 1)
            for w, dst in ((w0[0], w0s), (w0[1], w0b)):
                for r in range(REP):
                    k = r if r or dst is w0s else REP
                    act.dma_start(dst[F * r:F * r + F, k // REP:k // REP + len(range(k, SHIFTS, REP)), :],
                                  w[:, k:SHIFTS:REP, :]).then_inc(w0_in, 16)
            for q in range(3):
                act.dma_start(w1raw[:, 13 * q:13 * q + 13, :],
                              w1[13 * 128 * q:13 * 128 * (q + 1), :].rearrange("(i j) s -> j i s", j=128))\
                   .then_inc(w1_in[q], 16)

            def take_part(c, k):
                if k == 0:
                    act.wait_ge(xa_in, (c + 1) * 16 * REP)
                    act.activation(part, xa[:, :], ACT.Copy).then_inc(part_ready, 1)
                else:
                    act.wait_ge(rest_ready, c + 1)
                    act.activation(part, rest, ACT.Copy).then_inc(part_ready, 1)

            def finish_o0(c, par):
                await_unit(act, unit_used, (c - 1, TILE[-1]))
                for h in range(2):
                    act.activation(o0[:, par, h * HB:(h + 1) * HB], misc[:, h, :], ACT.Identity,
                                   bias=bias[:, 0:1]).then_inc(o0_ready, 1)

            def finish_o1(c):
                for h in range(2):
                    if h == 0:
                        act.wait_ge(half_summed, c + 1)
                    else:
                        await_unit(act, unit_used, (c, FIELD[-1]))
                    act.activation(o1[:, h * HB:(h + 1) * HB], o1_p[:, h * HB:(h + 1) * HB], ACT.Identity,
                                   bias=bias[:, 1:2]).then_inc(o1_ready, 1)

            def copy_turned(c, h):
                act.wait_ge(turned, 2 * c + h + 1)
                act.activation(o1t[:, 4 * h:4 * h + 4, :].rearrange("p g j -> p (g j)"), misc[:, h, :],
                               ACT.Copy).then_inc(o1t_ready, 1)

            def copy_g(c, par, pair, g):
                if g == 0 and par == 0:
                    act.wait_ge(gs_free, pair + 1)
                act.wait_ge(g_summed, c * NG + g + 1)
                at = par * CB + g * GB
                act.activation(gs[:, :, at:at + GB], misc[:, g % 2, 0:GB * FX].rearrange("p (b f) -> p f b", b=GB),
                               ACT.Copy).then_inc(g_ready, 1)

            def finish_y2(pair):
                act.wait_ge(y2_summed, pair + 1)
                act.activation(y2[:, :], misc[:, 0, 0:PB], ACT.Identity, bias=b2x[:, 0:1]).then_inc(y2_ready, 1)

            def chunk(c, par, pair):
                for i, k in enumerate(FIELD):
                    await_unit(act, z_ready, (c, k))
                    await_unit(act, unit_used, holder(ZHS, c, k))
                    act.activation(zh[:, ZHS[k], :], z[:, ZS[k], :], ACT.Copy).then_inc(zh_ready, 1)
                    if not first(c):
                        if i == ACT_O1:
                            finish_o1(c - 1)
                        if i in ACT_TURN:
                            copy_turned(c - 1, ACT_TURN[i])
                        if i in ACT_G:
                            copy_g(c - 1, 1 - par, pair, ACT_G[i])
                        if i == ACT_Y2 and par == 0:
                            finish_y2(pair)
                    if not last(c):
                        if i in ACT_X3:
                            take_part(c + 1, ACT_X3[i])
                        if i == ACT_O0:
                            finish_o0(c + 1, 1 - par)

            take_part(0, 0)
            for q in range(3):
                act.wait_ge(w1_in[q], 16)
                act.activation(w1h[:, 13 * q:13 * q + 13, :], w1raw[:, 13 * q:13 * q + 13, :], ACT.Copy)\
                   .then_inc(w1h_ready, 1)
                if q == 1:
                    take_part(0, 1)
            act.wait_ge(bias_in, 48)
            finish_o0(0, 0)
            act.wait_ge(b2_ready, 1)
            chunks(act, chunk)
            finish_o1(NCH - 1)
            for h in range(2):
                copy_turned(NCH - 1, h)
            for g in range(NG):
                copy_g(NCH - 1, 1, PAIRS - 1, g)
            finish_y2(PAIRS - 1)

        @block.vector
        def _(dve):
            def make_rest(c):
                if first(c):
                    dve.wait_ge(consts, 4 + REP + 1)
                dve.wait_ge(part_ready, 2 * c + 1)
                dve.scalar_tensor_tensor(out=rest, in0=part, scalar=minus[:, 0:1], in1=xa[:, :],
                                         op0=ALU.mult, op1=ALU.add).then_inc(rest_ready, 1)

            def make_x3(c, par):
                dve.wait_ge(part_ready, 2 * c + 2)
                dve.scalar_tensor_tensor(out=x3[:, par, :], in0=part, scalar=minus[:, 1:2], in1=rest,
                                         op0=ALU.mult, op1=ALU.add).then_inc(x3_ready, 1)

            def make_pairs(c, k):
                t = SEQ[k][1]
                p = rows_of(t)
                held = [u for u in range(NT) if u % XR == t % XR]
                loads = [16 * (rows_of(u) // F) for u in held]
                dve.wait_ge(xs_in[t % XR], (c + 1) * sum(loads) + sum(loads[:held.index(t) + 1]))
                if t == 0:
                    dve.wait_ge(xa_in, (c + 2) * 16 * REP)
                dve.tensor_tensor(z[0:p, ZS[k], :], xs[0:p, t % XR, :], xa[0:p, :], ALU.mult).then_inc(z_ready, 1)

            def make_product(c, par, k):
                i = SEQ[k][1]
                dve.wait_ge(xb_ready, c * F + i + 1)
                if i == 0:
                    dve.wait_ge(o0_ready, 2 * c + 2)
                dve.tensor_tensor(z[:, ZS[k], :], xb_p[(i + par) % 2][:, :], o0[:, par, :], ALU.mult)\
                   .then_inc(z_ready, 1)

            def chunk(c, par, pair):
                now = present(c)
                for n, k in enumerate(now + [None] * LOW_LAG):
                    if k is not None:
                        user = holder(ZS, c, k)
                        if user and user[1] in TILE:
                            await_unit(dve, unit_used, user)
                        elif user:
                            await_unit(dve, zh_ready, user, FIELD)
                            await_low(dve, user)
                        make_product(c, par, k) if SEQ[k][0] == "o1" else make_pairs(c, k)
                    if n >= LOW_LAG and now[n - LOW_LAG] in DVE_LOW:
                        make_low(dve, c, now[n - LOW_LAG], low_dve)
                    step = None if k is None or last(c) else \
                        {TILE[2]: 0, TILE[3]: 1}.get(k) if isinstance(c, int) and c < 0 else \
                        {FIELD[i]: n for i, n in DVE_X3.items()}.get(k)
                    if step == 0:
                        make_rest(c + 1)
                    if step == 1:
                        make_x3(c + 1, 1 - par)

            dve.wait_ge(w0_in, 16 * 2 * REP)
            for a, b, p in ((0, NT - 1, R3), (NT - 1, NT, rows_of(NT - 1))):
                dve.tensor_tensor(w0s[0:p, a:b, :], w0s[0:p, a:b, :], w0b[0:p, a:b, :], ALU.add).then_inc(w0_ready, 1)
            chunk(-1, 1, None)
            low_weights(dve, 0)
            dve.wait_ge(bias_in, 48)
            dve.tensor_scalar(b2x[:, :], bias[:, 2:3], float(D), None, ALU.mult).then_inc(b2_ready, 1)
            chunks(dve, chunk)

        @block.tensor
        def _(pe):
            def spread(c, par, i):
                if i == 0:
                    pe.wait_ge(x3_ready, c + 1)
                user = (c, FIELD[i - 2]) if i >= 2 else None if first(c) else (c - 1, FIELD[i - 2])
                await_unit(pe, z_ready, user)
                for h in range(2):
                    mm = pe.matmul(xb_p[(i + par) % 2][:, h * HB:(h + 1) * HB], pick[:, i, :],
                                   x3[:, par, h * HB:(h + 1) * HB], start=True, stop=True)
                mm.then_inc(xb_ready, 1)

            def layer1(c, i):
                k, start, stop = FIELD[i], i == 0, i == F - 1
                acc = [o1_p[:, h * HB:(h + 1) * HB] for h in range(2)]
                at = [slice(h * HB, (h + 1) * HB) for h in range(2)]
                if first(c) and i % 13 == 0:
                    pe.wait_ge(w1l_ready[i // 13], 1)
                await_unit(pe, zh_ready, (c, k), FIELD)

                def high(h):
                    if start and not first(c):
                        pe.wait_ge(o1_ready, 2 * c - 1 + h)
                    pe.matmul(acc[h], w1h[:, i, :], zh[:, ZHS[k], at[h]], start=start, stop=False)
                    pe.matmul(acc[h], w1l[:, i, :], zh[:, ZHS[k], at[h]], start=False, stop=False)

                def low(h):
                    return pe.matmul(acc[h], w1h[:, i, :], zl[:, ZLS[k], at[h]], start=False, stop=stop)

                high(0)
                if stop:
                    await_low(pe, (c, k))
                    low(0).then_inc(half_summed, 1)
                    high(1)
                else:
                    high(1)
                    await_low(pe, (c, k))
                    low(0)
                low(1).then_inc(unit_used, 1)

            def layer0(c, par, pair, t):
                p, k = rows_of(t), TILE[t]
                await_unit(pe, z_ready, (c, k))
                if t == 0 and pair is not None:
                    if par == 0:
                        pe.wait_ge(y2_ready, pair + 1)
                    pe.wait_ge(g_ready, c * NG)
                for h in range(2):
                    mm = pe.matmul(misc[:, h, :], w0s[0:p, t, :], z[0:p, ZS[k], h * HB:(h + 1) * HB],
                                   start=(t == 0), stop=(t == NT - 1))
                mm.then_inc(unit_used, 1)

            def turn(c, h):
                pe.wait_ge(o1_ready, 2 * c + h + 1)
                if h == 0 and not last(c):
                    pe.wait_ge(o0_ready, 2 * c + 4)
                for g in range(4):
                    k = (4 * h + g) * 128
                    mm = pe.transpose(misc[:, h, g * 128:(g + 1) * 128], o1[:, k:k + 128], ident[:, :])
                mm.then_inc(turned, 1)

            def g_sum(c, g):
                if g == 0:
                    pe.wait_ge(o1t_ready, 2 * c + 2)
                    pe.wait_ge(xd_in, (c + 1) * 16 * GB)
                if g >= 2:
                    pe.wait_ge(g_ready, c * NG + g - 1)
                pe.matmul(misc[:, g % 2, 0:GB * FX], o1t[:, g, :], xd[:, g, :, :].rearrange("p b f -> p (b f)"),
                          start=True, stop=True).then_inc(g_summed, 1)

            def layer2(c, fields):
                if fields[0] == 0:
                    pe.wait_ge(g_ready, (c + 1) * NG)
                for i in fields:
                    mm = pe.matmul(misc[:, 0, 0:PB], w2s[:, i, :], gs[:, i, :], start=(i == 0), stop=(i == F - 1))
                if fields[-1] == F - 1:
                    mm.then_inc(y2_summed, 1)

            def chunk(c, par, pair):
                now = present(c)
                for n, k in enumerate(now):
                    before_first = isinstance(c, int) and c < 0
                    if n + LEAD < len(now) and SEQ[now[n + LEAD]][0] == "o1":
                        spread(c, par, SEQ[now[n + LEAD]][1])
                    elif n + LEAD >= len(now) and not last(c) and not before_first:
                        spread(c + 1, 1 - par, n + LEAD - len(now))
                    what, i = SEQ[k]
                    if what == "o0":
                        layer0(c, par, pair, i)
                        continue
                    layer1(c, i)
                    if first(c) and i == F - 1:
                        pe.wait_ge(consts, 4 + REP + 2)
                        pe.wait_ge(ones_in, 16 * GB)
                        pe.wait_ge(w2_in, 16)
                    if not first(c):
                        if i in PE_TURN:
                            turn(c - 1, PE_TURN[i])
                        if i in PE_G:
                            g_sum(c - 1, PE_G[i])
                        if par == 0 and i in PE_LAYER2:
                            layer2(c - 1, PE_LAYER2[i])

            pe.wait_ge(w0_ready, 2)
            chunk(-1, 1, None)
            pe.wait_ge(picks, 1)
            for i in range(LEAD):
                spread(0, 0, i)
            chunks(pe, chunk)
            for h in range(2):
                turn(NCH - 1, h)
            for g in range(NG):
                g_sum(NCH - 1, g)
            layer2(NCH - 1, range(F))


def kernel(**inputs):
    import numpy as np
    import concourse.bacc as bacc
    from concourse.bass_utils import run_bass_kernel_spmd

    x = np.asarray(inputs["r_x"])
    by_field = np.ascontiguousarray(x.transpose(1, 0, 2).reshape(F, N))
    arrays = {
        "xr": np.concatenate([by_field, by_field[:SHIFTS]]),
        "xt": np.ascontiguousarray(x.transpose(0, 2, 1).reshape(N, F)),
    }
    w = np.asarray(inputs["L0_rec_w0"]).reshape(F, F, S)
    at, to = np.arange(F)[:, None], (np.arange(F)[:, None] + np.arange(SHIFTS)) % F
    arrays["w0"] = np.stack([w[at, to], w[to, at]])
    arrays["b0"] = np.ascontiguousarray(inputs["L0_rec_b0"])
    for k in (1, 2):
        arrays[f"w{k}"] = np.ascontiguousarray(inputs[f"L0_rec_w{k}"])
        arrays[f"b{k}"] = np.ascontiguousarray(inputs[f"L0_rec_b{k}"])
    nc = bacc.Bacc("TRN2", target_bir_lowering=False, num_devices=1)
    ap = {n: nc.dram_tensor(n, a.shape, mybir.dt.float32, kind="ExternalInput").ap() for n, a in arrays.items()}
    out = nc.dram_tensor("out", (2 * S, B), mybir.dt.float32, kind="ExternalOutput").ap()
    cin_kernel(nc, ap["xr"], ap["xt"], ap["w0"], ap["b0"], ap["w1"], ap["b1"], ap["w2"], ap["b2"], out)
    got = run_bass_kernel_spmd(nc, [arrays], core_ids=[0])
    return np.ascontiguousarray(got.results[0]["out"].T)
```
